# Optimizing a Trainium2 kernel written in Bass

```python
import numpy as np
import jax
import jax.numpy as jnp

def _softmax(x, axis=-1):
    return jax.nn.softmax(x, axis=axis)

def _gelu(x):
    return jax.nn.gelu(x, approximate=True)

def _silu(x):
    return jax.nn.silu(x)

def _sigmoid(x):
    return jax.nn.sigmoid(x)

def _layernorm(x, axis=-1, eps=1e-05):
    m = jnp.mean(x, axis=axis, keepdims=True)
    v = jnp.var(x, axis=axis, keepdims=True)
    return (x - m) / jnp.sqrt(v + eps)

def _scatter_add(tgt, idx, src, axis=0):
    return tgt.at[idx].add(src)

def _segment_sum(src, seg, n):
    return jax.ops.segment_sum(src, seg, n)
kernel_name = 'mk_gnn_preln_d1_gnn_r8_691f4c'

def setup_inputs(seed: int=0):
    np.random.seed(seed)
    _w = jnp.asarray

    def _rec_inputs():
        import jax
        import jax.numpy as jnp
        _gk = jax.random.key(seed)
        x = -0.0002117 + 1 * jax.random.normal(jax.random.fold_in(_gk, 1), (6250, 512), jnp.float32)
        src = jax.random.randint(jax.random.fold_in(_gk, 2), (100000,), 0, 6250, jnp.int32)
        dst = jax.random.randint(jax.random.fold_in(_gk, 3), (100000,), 0, 6250, jnp.int32)
        _o = jnp.argsort(dst, stable=True)
        src = src[_o]
        dst = dst[_o]
        return (x, src, dst)
    x, src, dst = _rec_inputs()

    def _L0_gnn_setup():
        import jax, jax.numpy as jnp
        import numpy as np
        N = 6250
        E = 50000
        D = 512
        L = 3
        INNER = (L + 1) * D
        EPS = 1e-05

        def _gcn_conv(x, W, b, src, dst):
            h = x @ W
            deg = jnp.zeros((N,), x.dtype).at[dst].add(1.0) + 1.0
            dinv = jax.lax.rsqrt(deg)
            norm = dinv[src] * dinv[dst]
            agg = jnp.zeros_like(h).at[dst].add(h[src] * norm[:, None])
            agg = agg + h * (dinv * dinv)[:, None]
            return agg + b
        key = jax.random.key(seed)
        ks = jax.random.split(key, 6)
        x = jax.random.normal(ks[0], (N, D), dtype=jnp.float32)
        edge_index = jax.random.randint(ks[1], (2, E), 0, N, dtype=jnp.int64)
        Ws = jax.random.normal(ks[2], (L, D, D), dtype=jnp.float32) / np.float32(np.sqrt(D))
        bs = jnp.zeros((L, D), jnp.float32)
        bn_gamma = jnp.ones((INNER,), jnp.float32)
        bn_beta = jnp.zeros((INNER,), jnp.float32)
        out_W = jax.random.normal(ks[3], (INNER, D), dtype=jnp.float32) / np.float32(np.sqrt(INNER))
        out_b = jnp.zeros((D,), jnp.float32)
        return {'x': x, 'edge_index': edge_index, 'Ws': Ws, 'bs': bs, 'bn_gamma': bn_gamma, 'bn_beta': bn_beta, 'out_W': out_W, 'out_b': out_b}
    _L0_gnn_all = _L0_gnn_setup()
    _L0_gnn_in = {k: v for k, v in _L0_gnn_all.items() if k in ('Ws', 'bs', 'bn_gamma', 'bn_beta', 'out_W', 'out_b')}
    del _L0_gnn_all
    return {'x': x, 'src': src, 'dst': dst, 'L0_gnn_Ws': _L0_gnn_in['Ws'], 'L0_gnn_bs': _L0_gnn_in['bs'], 'L0_gnn_bn_gamma': _L0_gnn_in['bn_gamma'], 'L0_gnn_bn_beta': _L0_gnn_in['bn_beta'], 'L0_gnn_out_W': _L0_gnn_in['out_W'], 'L0_gnn_out_b': _L0_gnn_in['out_b']}

def reference(x, src, dst, L0_gnn_Ws, L0_gnn_bs, L0_gnn_bn_gamma, L0_gnn_bn_beta, L0_gnn_out_W, L0_gnn_out_b):
    import jax
    import jax.numpy as jnp

    def _L0_gnn_ref(x, edge_index, Ws, bs, bn_gamma, bn_beta, out_W, out_b):
        import jax, jax.numpy as jnp
        import numpy as np
        N = 6250
        E = 50000
        D = 512
        L = 3
        INNER = (L + 1) * D
        EPS = 1e-05

        def _gcn_conv(x, W, b, src, dst):
            h = x @ W
            deg = jnp.zeros((N,), x.dtype).at[dst].add(1.0) + 1.0
            dinv = jax.lax.rsqrt(deg)
            norm = dinv[src] * dinv[dst]
            agg = jnp.zeros_like(h).at[dst].add(h[src] * norm[:, None])
            agg = agg + h * (dinv * dinv)[:, None]
            return agg + b
        src, dst = (edge_index[0], edge_index[1])
        h = x
        x_cat = [x]
        for l in range(L):
            h = jax.nn.gelu(_gcn_conv(h, Ws[l], bs[l], src, dst), approximate=False)
            x_cat.append(h)
        xc = jnp.concatenate(x_cat, axis=-1)
        mean = jnp.mean(xc, axis=0)
        var = jnp.var(xc, axis=0)
        xn = (xc - mean) * jax.lax.rsqrt(var + EPS) * bn_gamma + bn_beta
        return xn @ out_W + out_b
    edge_index = jnp.stack([src, dst])
    h = jnp.maximum(_layernorm(x, axis=-1), 0.0)
    x = x + _L0_gnn_ref(h, edge_index, L0_gnn_Ws, L0_gnn_bs, L0_gnn_bn_gamma, L0_gnn_bn_beta, L0_gnn_out_W, L0_gnn_out_b)
    return x

_drawn_inputs = setup_inputs


def setup_inputs(seed=0):
    import zlib

    import numpy as np

    out = dict(_drawn_inputs(seed))
    spreads = {'L0_gnn_bs': (0.0, 0.1),
     'L0_gnn_bn_gamma': (1.0, 0.2),
     'L0_gnn_bn_beta': (0.0, 0.1),
     'L0_gnn_out_b': (0.0, 0.1)}
    factors = {}
    for name, (base, spread) in spreads.items():
        noise = np.random.default_rng([zlib.crc32(name.encode()), seed]).standard_normal(out[name].shape)
        drawn = base * np.exp(spread * noise) if base else spread * noise
        out[name] = jnp.asarray(drawn.astype(out[name].dtype))
    for name, factor in factors.items():
        out[name] = (out[name] * factor).astype(out[name].dtype)
    return out
```

```python
from contextlib import ExitStack

import concourse.bass as bass
from concourse import mybir

ALU = mybir.AluOpType
ACT = mybir.ActivationFunctionType
AX_X = mybir.AxisListType.X
F32 = mybir.dt.float32
F16 = mybir.dt.float16
BF16 = mybir.dt.bfloat16
I32 = mybir.dt.int32


def gnn_kernel(
    nc: bass.Bass,
    x: bass.AP,
    src: bass.AP,
    dst: bass.AP,
    Ws: bass.AP,
    bs: bass.AP,
    gamma: bass.AP,
    beta: bass.AP,
    out_W: bass.AP,
    out_b: bass.AP,
    out: bass.AP,
):
    P = 128
    N, D = x.shape
    (E,) = src.shape
    L = Ws.shape[0]
    KC = D // P
    BN = 125
    NB = N // BN
    NT = -(-E // P)
    RING = 16
    SRING = 8
    STEPS = -(-(NT + NB - 1) // (2 * RING)) * 2 * RING
    SC = -(-STEPS // P)
    ROW = 2 * D + 16
    SCALE_AT = D
    EP = 125
    EC = E // EP
    HCH = 16
    NCH = EC // HCH
    assert N == NB * BN and E == EP * EC and EC % (2 * HCH) == 0 and D == KC * P
    assert KC * BN <= 512 and NB % 2 == 0 and STEPS <= SC * P
    LN_EPS = BN_EPS = 1e-5
    ROUND = 12582912.0
    NO_NODE = 100000.0 * 4
    PARTS = L + 1

    def dram(name, shape, dt):
        return nc.dram_tensor(name, shape, dt, kind="Internal").ap()

    row_table = [dram(f"row_table{n}", (NB * P, ROW), F16) for n in range(2)]
    hT_dram = [dram(f"hT_dram{n}", (NB, P, KC * BN), F32) for n in range(2)]
    y_dram = dram("y_dram", (NB, P, D), F32)
    edge_dst = dram("edge_dst", (NT * P, 1), I32)
    edge_src = dram("edge_src", (NT * P, 1), I32)
    out_w_v = out_W.rearrange("(k c p) n -> k p c n", p=P, c=KC)
    w_v = Ws.rearrange("l (c p) n -> l p c n", p=P)
    x_v = x.rearrange("(b p) n -> b p n", p=BN)
    out_v = out.rearrange("(b p) n -> b p n", p=BN)

    with ExitStack() as ctx:
        def sb(name, shape, dt=F32, stack=ctx):
            return stack.enter_context(nc.sbuf_tensor(name, shape, dt))

        def pb(name, shape):
            return ctx.enter_context(nc.psum_tensor(name, shape, F32))

        def sem(name):
            return ctx.enter_context(nc.semaphore(name))

        hcur = sb("hcur", [P, NB * D])
        idx = sb("idx", [P, SC * P], I32)
        dloc = sb("dloc", [P, SC * P])
        h_sb = sb("h_sb", [P, D])
        rowbuf = sb("rowbuf", [P, 2 * ROW], F16)
        hT_out = sb("hT_out", [P, 2 * KC * BN])
        y_out = sb("y_out", [P, 2 * D])
        const_bc = sb("const_bc", [P, D])
        bnst = sb("bnst", [P, KC, NB * 6])
        dinv = sb("dinv", [P, NB])
        ident = sb("ident", [P, P])
        iota_l = sb("iota_l", [P, P])
        zeros = sb("zeros", [P, D], BF16)
        ones = sb("ones", [P, P])
        mv = sb("mv", [P, KC, 2])
        gb = sb("gb", [P, 2, PARTS * KC])
        sc4 = sb("sc4", [P, 6, KC])
        rowmax = sb("rowmax", [P, 1])
        expo = sb("expo", [P, 3], I32)
        ends = sb("ends", [1, NB + 1], I32)
        idx_stage = sb("idx_stage", [P, 2 * RING], I32)
        ln_mv = sb("ln_mv", [P, NB, 2])
        ln_r = sb("ln_r", [P, 5, NB])
        wo = sb("wo", [P, KC, D])
        wo_s = sb("wo_s", [P, KC, D])

        with ExitStack() as graph:
            def gsb(name, shape, dt=F32):
                return sb(name, shape, dt, graph)

            ln_st = gsb("ln_st", [P, NB, 6])
            dst_i = gsb("dst_i", [EP, EC + 1], I32)
            src_i = gsb("src_i", [EP, EC], I32)
            dst_f = gsb("dst_f", [EP, EC + 1])
            blk = gsb("blk", [EP, EC])
            tmp_e = gsb("tmp_e", [EP, EC])
            blk_h = gsb("blk_h", [EP, EC], BF16)
            lane_h = gsb("lane_h", [EP, EC], BF16)
            hist = gsb("hist", [EP, NB + 1])
            cnt = gsb("cnt", [P, NB + 1])
            rows_b = gsb("rows_b", [P, 8, NB])
            cmp3 = gsb("cmp3", [P, SC, NB])
            p_of = gsb("p_of", [P, SC])
            step_b = gsb("step_b", [P, 4, SC])
            tile_of = gsb("tile_of", [P, SC], I32)
            unsorted = gsb("unsorted", [1, 1], I32)
            fill_i = gsb("fill_i", [1, 2, NT * P - E], I32)
            sort_off = gsb("sort_off", [EP, 2])
            stage_pos = gsb("stage_pos", [EP, 1], I32)
            stage_dst = gsb("stage_dst", [EP, 1], I32)
            stage_src = gsb("stage_src", [EP, 1], I32)
            upper = gsb("upper", [EP, EP])
            with ExitStack() as counting:
                iota_lane = sb("iota_lane", [EP, BN, HCH], BF16, counting)
                iota_blk = sb("iota_blk", [EP, NB, HCH], BF16, counting)
                eq_lane = sb("eq_lane", [EP, 2, BN, HCH], BF16, counting)
                eq_blk = sb("eq_blk", [EP, 2, NB, HCH], BF16, counting)
            tile_dst = gsb("tile_dst", [P, SC, P], I32)
            tile_src = gsb("tile_src", [P, SC, P], I32)
            step_dst = gsb("step_dst", [P, SC, P])
            step_src = gsb("step_src", [P, SC, P])
            step_q = gsb("step_q", [P, SC, P])
        ring = sb("ring", [P, RING * ROW], F16)
        smat = sb("smat", [P, SRING * P], BF16)
        u_sb = sb("u_sb", [P, D])
        uT_sb = sb("uT_sb", [P, KC * BN])
        wl = sb("wl", [P, KC, D])
        bias_bc = sb("bias_bc", [P, D])
        hT_in = sb("hT_in", [P, 2 * KC * BN])
        y_in = sb("y_in", [P, 2 * D])

        agg = pb("agg", [P, 2 * D])
        ps_u = pb("ps_u", [P, D])
        ps_z = pb("ps_z", [P, D])
        ps_t = pb("ps_t", [P, D])
        ps_y = pb("ps_y", [P, 2 * D])
        ps_c = pb("ps_c", [P, D])

        edges_loaded = sem("edges_loaded")
        edges_copied = sem("edges_copied")
        consts = sem("consts")
        eq_ready = sem("eq_ready")
        eq_used = sem("eq_used")
        hist_done = sem("hist_done")
        hist_copied = sem("hist_copied")
        cnt_done = sem("cnt_done")
        flag_ready = sem("flag_ready")
        rows_b_ready = sem("rows_b_ready")
        sort_scanned = sem("sort_scanned")
        sort_offset = sem("sort_offset")
        sort_chain = sem("sort_chain")
        sort_done = sem("sort_done")
        pool_chain = sem("pool_chain")
        staged = sem("staged")
        scattered = sem("scattered")
        tiles_known = sem("tiles_known")
        tiles_fetched = [sem(f"tiles_fetched{n}") for n in range(2)]
        steps_made = sem("steps_made")
        steps_turned = sem("steps_turned")
        tables_ready = sem("tables_ready")
        deg_ready = sem("deg_ready")
        root_ready = sem("root_ready")
        chain = sem("chain")
        x_loaded = [sem(f"x_loaded{n}") for n in range(NB // 7 + 1)]
        ln_ready = sem("ln_ready")
        idx_ready = sem("idx_ready")
        gathered = [sem(f"gathered{n}") for n in range(RING)]
        slot_free = sem("slot_free")
        landed = sem("landed")
        s_ready = sem("s_ready")
        steps_done = sem("steps_done")
        agg_done = sem("agg_done")
        u_ready = sem("u_ready")
        u_turned = sem("u_turned")
        uT_ready = sem("uT_ready")
        z_done = sem("z_done")
        z_ready = sem("z_ready")
        h_ready = sem("h_ready")
        hp_ready = sem("hp_ready")
        scale_steps = sem("scale_steps")
        hi_ready = sem("hi_ready")
        lo_ready = sem("lo_ready")
        rows_stored = sem("rows_stored")
        h_turned = sem("h_turned")
        stats_done = sem("stats_done")
        hT_ready = sem("hT_ready")
        hT_stored = sem("hT_stored")
        hT_loaded = sem("hT_loaded")
        y_loaded = sem("y_loaded")
        y_done = sem("y_done")
        y_ready = sem("y_ready")
        y_stored = sem("y_stored")
        w_loaded = sem("w_loaded")
        b_loaded = sem("b_loaded")
        wo_loaded = sem("wo_loaded")
        small_loaded = sem("small_loaded")
        bn_var = sem("bn_var")
        bn_root = sem("bn_root")
        bn_shift = sem("bn_shift")
        const_done = sem("const_done")
        ws_ready = sem("ws_ready")
        h3_ready = sem("h3_ready")
        out_part = sem("out_part")

        block = ctx.enter_context(nc.Block())

        def wait(eng, s, value):
            if not isinstance(value, int) or value > 0:
                eng.wait_ge(s, value)

        def live(j):
            return not isinstance(j, int) or 0 <= j < NB

        def pipeline(eng, iteration, lag, head=0):
            head = max(head, lag)
            for i in range(head):
                iteration(i)
            with eng.Fori(head, NB) as i:
                iteration(i)
            for i in range(NB, NB + lag):
                iteration(i)

        def blk_cols(t, j, width=D, used=D):
            return t[:, bass.ds(j * width, used)]

        @block.sync
        def _(sp):
            sp.dma_start(dst_i[0:EP - 1, :], bass.AP(dst.tensor, 0, [[EC, EP - 1], [1, EC + 1]])
                         ).then_inc(edges_loaded, 16)
            sp.dma_start(dst_i[EP - 1:EP, 0:EC], bass.AP(dst.tensor, (EP - 1) * EC, [[EC, 1], [1, EC]])
                         ).then_inc(edges_loaded, 16)
            sp.dma_start(dst_i[EP - 1:EP, EC:EC + 1], bass.AP(dst.tensor, E - 1, [[1, 1], [1, 1]])
                         ).then_inc(edges_loaded, 16)
            sp.dma_start(src_i[:, :], src.rearrange("(p c) -> p c", p=EP)).then_inc(edges_loaded, 16)
            for n in range(NB // 7):
                sp.dma_start(hcur[:, n * 7 * D:(n + 1) * 7 * D].rearrange("p (b n) -> p b n", b=7),
                             bass.AP(x.tensor, n * 7 * BN * D, [[D, P], [BN * D, 7], [1, D]])
                             ).then_inc(x_loaded[n], 16)
            sp.dma_start(hcur[0:BN, (NB - 1) * D:NB * D], x_v[NB - 1]).then_inc(x_loaded[NB // 7], 16)
            for s_in, s_out in ((dst, edge_dst), (src, edge_src)):
                sp.dma_start(s_out[0:E, :].rearrange("(p c) o -> p (c o)", p=EP),
                             s_in.rearrange("(p c) -> p c", p=EP)).then_inc(edges_copied, 16)
            sp.wait_ge(consts, 1)
            for n, s_out in enumerate((edge_dst, edge_src)):
                sp.dma_start(s_out[E:NT * P, :].rearrange("(a c) o -> a (c o)", a=1), fill_i[:, n, :]
                             ).then_inc(edges_copied, 16)
            for l in range(L):
                with sp.Fori(0, STEPS // RING) as r:
                    for n in range(RING):
                        sp.wait_ge(gathered[n], r * 16 + 16 * (l * (STEPS // RING) + 1))
                        sp.sem_inc(landed, 1)

        @block.gpsimd
        def _(pool):
            links = [0]

            def link(ins):
                links[0] += 1
                ins.then_inc(pool_chain, 1)
                pool.wait_ge(pool_chain, links[0])

            G = nc.gpsimd
            iota = dict(base=0, allow_small_or_imprecise_dtypes=True)
            link(G.memset(fill_i[:, 0, :], int(NO_NODE)))
            G.memset(fill_i[:, 1, :], 0).then_inc(consts, 1)
            pool.wait_ge(consts, 1)
            link(G.iota(iota_l[:, :], [[1, P]], channel_multiplier=0, **iota))
            link(G.iota(iota_lane[:, :, :], [[1, BN], [0, HCH]], channel_multiplier=0, **iota))
            link(G.iota(iota_blk[:, :, :], [[1, NB], [0, HCH]], channel_multiplier=0, **iota))
            link(G.memset(zeros[:, :], 0.0))
            link(G.memset(ones[:, :], 1.0))
            link(G.memset(ident[:, :], 0.0))
            G.affine_select(out=ident[:, :], in_=ident[:, :], compare_op=ALU.not_equal, fill=1.0,
                            base=0, pattern=[[-1, P]], channel_multiplier=1).then_inc(consts, 1)
            pool.wait_ge(consts, 2)
            link(G.affine_select(out=upper[:, :], in_=ones[0:EP, 0:EP], compare_op=ALU.is_gt, fill=0.0,
                                 base=0, pattern=[[1, EP]], channel_multiplier=-1))
            link(G.iota(p_of[:, :], [[P, SC]], channel_multiplier=1, **iota))
            link(G.memset(rowbuf[:, :], 0.0))
            G.memset(y_out[:, :], 0.0).then_inc(consts, 1)
            pool.wait_ge(consts, 3)

            pool.wait_ge(flag_ready, 1)
            pool.wait_ge(edges_copied, 4 * 16)
            with pool.If(pool.value_load(unsorted[0:1, 0:1], min_val=0, max_val=1) > 0):
                pool.wait_ge(sort_done, 1)
                with pool.Fori(0, EC) as c:
                    for n, (stage, col) in enumerate(((stage_pos, blk[:, bass.ds(c, 1)].bitcast(I32)),
                                                      (stage_dst, dst_i[:, bass.ds(c, 1)]),
                                                      (stage_src, src_i[:, bass.ds(c, 1)]))):
                        G.tensor_copy(stage[:, :], col).then_inc(staged, 1)
                        pool.wait_ge(staged, c * 3 + n + 1)
                    pool.sem_inc(slot_free, 1)
                    for s_out, staged_val in ((edge_dst, stage_dst), (edge_src, stage_src)):
                        nc.gpsimd.indirect_dma_start(
                            out=s_out, out_offset=bass.IndirectOffsetOnAxis(ap=stage_pos[:, :], axis=0),
                            in_=staged_val[:, :], in_offset=None).then_inc(scattered, 16)
                    pool.wait_ge(scattered, c * 32 + 32)

            pool.wait_ge(tiles_known, 1)
            for n, (table, fetched) in enumerate(((edge_dst, tile_dst), (edge_src, tile_src))):
                for c in range(SC):
                    nc.gpsimd.indirect_dma_start(
                        out=fetched[:, c, :], out_offset=None, in_=table.rearrange("(t p) o -> t (p o)", p=P),
                        in_offset=bass.IndirectOffsetOnAxis(ap=tile_of[:, c:c + 1], axis=0)
                    ).then_inc(tiles_fetched[n], 16)

            pool.wait_ge(tables_ready, 1)
            for l in range(L):
                pool.wait_ge(rows_stored, 16 * NB * (l + 1))
                with pool.Fori(0, STEPS // (2 * RING)) as two:
                    for m in range(2):
                        first = two * (2 * RING) + (l * STEPS + m * RING)
                        pool.wait_ge(steps_done, first + 1)
                        pool.sem_inc(slot_free, 1)
                        G.tensor_copy(idx_stage[:, m * RING:(m + 1) * RING],
                                      idx[:, bass.ds(two * (2 * RING) + m * RING, RING)]).then_inc(idx_ready, 1)
                        pool.wait_ge(idx_ready, two * 2 + (l * (STEPS // RING) + m + 1))
                        for n in range(RING):
                            pool.wait_ge(steps_done, first + n + 1)
                            pool.sem_inc(slot_free, 1)
                            G.indirect_dma_start(
                                out=ring[:, n * ROW:(n + 1) * ROW], out_offset=None, in_=row_table[l % 2],
                                in_offset=bass.IndirectOffsetOnAxis(
                                    ap=idx_stage[:, m * RING + n:m * RING + n + 1], axis=0)
                            ).then_inc(gathered[n], 16)

        @block.vector
        def _(dve):
            links = [0]

            def link(ins):
                links[0] += 1
                ins.then_inc(chain, 1)
                dve.wait_ge(chain, links[0])

            V = nc.vector

            def refine(r, v, t):
                link(V.tensor_tensor(t, r, r, ALU.mult))
                link(V.tensor_tensor(t, t, v, ALU.mult))
                link(V.tensor_scalar(t, t, -0.5, 1.5, ALU.mult, ALU.add))
                link(V.tensor_tensor(r, r, t, ALU.mult))

            dve.wait_ge(edges_loaded, 4 * 16)
            dve.wait_ge(consts, 2)
            dve.wait_ge(consts, 3)
            link(V.tensor_copy(dst_f[:, :], dst_i[:, :]))
            link(V.tensor_scalar(tmp_e[:, :], dst_f[:, 0:EC], 1.0 / BN, -0.496, ALU.mult, ALU.add))
            link(V.tensor_scalar(blk[:, :], tmp_e[:, :], ROUND, ROUND, ALU.add, ALU.subtract))
            link(V.scalar_tensor_tensor(lane_h[:, :], blk[:, :], -float(BN), dst_f[:, 0:EC], ALU.mult, ALU.add))
            link(V.tensor_copy(blk_h[:, :], blk[:, :]))
            link(V.tensor_tensor(tmp_e[:, :], dst_f[:, 1:EC + 1], dst_f[:, 0:EC], ALU.is_lt))
            link(V.tensor_reduce(hist[:, NB:NB + 1], tmp_e[:, :], AX_X, ALU.add))

            with dve.Fori(0, NCH // 2) as pair:
                for n in range(2):
                    dve.wait_ge(eq_used, pair * 2 + n + 1)
                    at = (pair * 2 + n) * HCH
                    V.tensor_tensor(eq_blk[:, n, :, :],
                                    blk_h[:, bass.ds(at, HCH)].unsqueeze(1).to_broadcast([EP, NB, HCH]),
                                    iota_blk[:, :, :], ALU.is_equal)
                    V.tensor_tensor(eq_lane[:, n, :, :],
                                    lane_h[:, bass.ds(at, HCH)].unsqueeze(1).to_broadcast([EP, BN, HCH]),
                                    iota_lane[:, :, :], ALU.is_equal).then_inc(eq_ready, 1)
            dve.wait_ge(hist_done, 1)
            link(V.tensor_copy(hist[:, 0:NB], ps_c[0:EP, 0:NB]))
            V.tensor_scalar(dinv[0:BN, :], hist[:, 0:NB], 1.0, None, ALU.add).then_inc(deg_ready, 1)
            V.tensor_copy(cnt[0:1, 0:1], hist[0:1, 0:1]).then_inc(hist_copied, 1)

            p_incl, p_excl, t_first, t_end, n_steps, e_incl, shift, spare = (rows_b[:, n, :] for n in range(8))
            dve.wait_ge(cnt_done, 1)
            link(V.tensor_copy(cnt[:, :], ps_c[:, 64:64 + NB + 1]))
            V.tensor_scalar(unsorted[0:1, 0:1], cnt[0:1, NB:NB + 1], 1.0, None, ALU.min).then_inc(flag_ready, 1)
            link(V.tensor_tensor_scan(p_incl, ones[:, 0:NB], cnt[:, 0:NB], 0.0, ALU.mult, ALU.add))
            link(V.tensor_tensor(p_excl, p_incl, cnt[:, 0:NB], ALU.subtract))

            dve.wait_ge(flag_ready, 1)
            pos, scan = (wo_s[0:EP, :, :].rearrange("p c n -> p (c n)")[:, n * EC:(n + 1) * EC] for n in range(2))
            with dve.If(dve.value_load(unsorted[0:1, 0:1], min_val=0, max_val=1) > 0):
                V.memset(pos, 0.0).then_inc(sort_chain, 1)
                with dve.Fori(0, NB) as b:
                    dve.wait_ge(sort_chain, b * 5 + 1)
                    V.tensor_scalar(tmp_e[:, :], blk_h[:, :], iota_l[0:EP, bass.ds(b, 1)], None, ALU.is_equal
                                    ).then_inc(sort_chain, 1)
                    dve.wait_ge(sort_chain, b * 5 + 2)
                    V.tensor_tensor_scan(scan, tmp_e[:, :], tmp_e[:, :], 0.0, ALU.bypass, ALU.add
                                         ).then_inc(sort_scanned, 1)
                    dve.wait_ge(sort_offset, b + 1)
                    V.tensor_scalar(sort_off[:, 0:1], ps_z[0:EP, 0:1], p_excl[0:EP, bass.ds(b, 1)], -1.0,
                                    ALU.add, ALU.add).then_inc(sort_chain, 1)
                    dve.wait_ge(sort_chain, b * 5 + 3)
                    V.tensor_scalar(scan, scan, sort_off[:, 0:1], None, ALU.add).then_inc(sort_chain, 1)
                    dve.wait_ge(sort_chain, b * 5 + 4)
                    V.tensor_tensor(scan, scan, tmp_e[:, :], ALU.mult).then_inc(sort_chain, 1)
                    dve.wait_ge(sort_chain, b * 5 + 5)
                    V.tensor_tensor(pos, pos, scan, ALU.add).then_inc(sort_chain, 1)
                dve.wait_ge(sort_chain, NB * 5 + 1)
                V.tensor_copy(blk[:, :].bitcast(I32), pos).then_inc(sort_done, 1)

            link(V.tensor_scalar(t_first, p_excl, 1.0 / P, -0.498, ALU.mult, ALU.add))
            link(V.tensor_scalar(t_first, t_first, ROUND, ROUND, ALU.add, ALU.subtract))
            link(V.tensor_scalar(t_end, p_incl, 1.0 / P, 0.498, ALU.mult, ALU.add))
            link(V.tensor_scalar(t_end, t_end, ROUND, ROUND, ALU.add, ALU.subtract))
            link(V.tensor_tensor(n_steps, t_end, t_first, ALU.subtract))
            link(V.tensor_scalar(n_steps, n_steps, 1.0, None, ALU.max))
            link(V.tensor_tensor_scan(e_incl, ones[:, 0:NB], n_steps, 0.0, ALU.mult, ALU.add))
            link(V.tensor_tensor(shift, e_incl, n_steps, ALU.subtract))
            link(V.tensor_tensor(shift, shift, t_first, ALU.subtract))
            link(V.memset(ends[:, :], 0))
            link(V.tensor_copy(ends[0:1, 1:NB], e_incl[0:1, 0:NB - 1]))
            link(V.memset(ends[:, NB:NB + 1], STEPS))
            b_of, sh_of, t_of, b_first = (step_b[:, n, :] for n in range(4))
            link(V.tensor_tensor(cmp3[:, :, :], e_incl.unsqueeze(1).to_broadcast([P, SC, NB]),
                                 p_of[:, :].unsqueeze(2).to_broadcast([P, SC, NB]), ALU.is_le))
            link(V.tensor_reduce(b_of, cmp3[:, :, :], AX_X, ALU.add))
            link(V.tensor_tensor(cmp3[:, :, :], iota_l[:, 0:NB].unsqueeze(1).to_broadcast([P, SC, NB]),
                                 b_of.unsqueeze(2).to_broadcast([P, SC, NB]), ALU.is_equal))
            link(V.tensor_tensor(cmp3[:, :, :], cmp3[:, :, :], shift.unsqueeze(1).to_broadcast([P, SC, NB]),
                                 ALU.mult))
            link(V.tensor_reduce(sh_of, cmp3[:, :, :], AX_X, ALU.add))
            link(V.tensor_tensor(t_of, p_of[:, :], sh_of, ALU.subtract))
            link(V.tensor_scalar(b_first, b_of, float(BN), None, ALU.mult))
            V.tensor_scalar(tile_of[:, :], t_of, float(NT - 1), None, ALU.min).then_inc(tiles_known, 1)

            dve.wait_ge(root_ready, 1)
            deg, root, newton = (ln_r[0:BN, n, :] for n in range(3))
            link(V.tensor_copy(deg, dinv[0:BN, :]))
            link(V.reciprocal(dinv[0:BN, :], root))
            refine(dinv[0:BN, :], deg, newton)

            for n in range(NB // 7 + 1):
                dve.wait_ge(x_loaded[n], 16)
                for j in range(n * 7, min((n + 1) * 7, NB)):
                    last = V.bn_stats(ln_st[0:BN, j, :], hcur[0:BN, j * D:(j + 1) * D])
            link(last)
            for j in range(NB):
                last = V.bn_aggr(ln_mv[0:BN, j, :], ln_st[0:BN, j, :])
            link(last)
            mean, var = (ln_mv[0:BN, :, n] for n in range(2))
            v_eps, root, rstd, nbias, newton = (ln_r[0:BN, n, :] for n in range(5))
            V.tensor_scalar(v_eps, var, LN_EPS, None, ALU.add).then_inc(deg_ready, 1)
            dve.wait_ge(root_ready, 2)
            link(V.reciprocal(rstd, root))
            refine(rstd, v_eps, newton)
            V.scalar_tensor_tensor(nbias, mean, -1.0, rstd, ALU.mult, ALU.mult).then_inc(ln_ready, 1)

            dve.wait_ge(tiles_fetched[0], SC * 16)
            for c in range(SC):
                V.tensor_scalar(step_dst[:, c, :], tile_dst[:, c, :], b_first[:, c:c + 1], None, ALU.subtract)
            dve.wait_ge(tiles_fetched[1], SC * 16)
            link(V.tensor_copy(step_src[:, :, :], tile_src[:, :, :]))
            link(V.tensor_scalar(step_q[:, :, :], step_src[:, :, :], 1.0 / BN, -0.496, ALU.mult, ALU.add))
            link(V.tensor_scalar(step_q[:, :, :], step_q[:, :, :], ROUND, ROUND, ALU.add, ALU.subtract))
            V.scalar_tensor_tensor(step_src[:, :, :], step_q[:, :, :], float(P - BN), step_src[:, :, :],
                                   ALU.mult, ALU.add).then_inc(steps_made, 1)
            dve.wait_ge(steps_turned, 1)
            V.tensor_copy(dloc[:, :], agg[:, 0:SC * P])
            V.tensor_copy(idx[:, :], ps_y[:, 0:SC * P]).then_inc(tables_ready, 1)

            def scale_rows(l, j):
                g = l * NB + j
                dve.wait_ge(h_ready, g + 1)
                wait(dve, rows_stored, (g - 1) * 16)
                wait(dve, hi_ready, g)
                hp = hcur[0:BN, bass.ds(j * D, D)]
                if l == 0:
                    V.tensor_scalar(hp, h_sb[0:BN, :], dinv[0:BN, bass.ds(j, 1)], 0.0, ALU.mult, ALU.max,
                                    accum_out=rowmax[0:BN, :]).then_inc(scale_steps, 2)
                else:
                    V.tensor_reduce(rowmax[0:BN, :], h_sb[0:BN, :], AX_X, ALU.max, apply_absolute_value=True
                                    ).then_inc(scale_steps, 1)
                    V.tensor_scalar(hp, h_sb[0:BN, :], dinv[0:BN, bass.ds(j, 1)], None, ALU.mult)
                    dve.wait_ge(scale_steps, g * 5 + 1)
                    V.tensor_scalar(rowmax[0:BN, :], rowmax[0:BN, :], dinv[0:BN, bass.ds(j, 1)], None, ALU.mult
                                    ).then_inc(scale_steps, 1)
                dve.wait_ge(scale_steps, g * 5 + 2)
                V.tensor_scalar(expo[0:BN, 0:1], rowmax[0:BN, :].bitcast(I32), 23, None,
                                ALU.logical_shift_right).then_inc(scale_steps, 1)
                dve.wait_ge(scale_steps, g * 5 + 3)
                V.tensor_scalar(expo[0:BN, 1:2], expo[0:BN, 0:1], 15.0, 14.0, ALU.max, ALU.subtract
                                ).then_inc(scale_steps, 1)
                dve.wait_ge(scale_steps, g * 5 + 4)
                V.tensor_scalar(expo[0:BN, 2:3], expo[0:BN, 1:2], -1.0, 254.0, ALU.mult, ALU.add
                                ).then_inc(scale_steps, 1)
                dve.wait_ge(scale_steps, g * 5 + 5)
                V.tensor_scalar(rowbuf[0:BN, :].bitcast(I32)[:, bass.ds((j & 1) * (ROW // 2) + SCALE_AT, 2)],
                                expo[0:BN, 1:3], 23, None, ALU.logical_shift_left).then_inc(hp_ready, 1)

            def low_part(l, j):
                g = l * NB + j
                dve.wait_ge(hi_ready, g + 1)
                half = (j & 1) * ROW
                c = rowbuf[0:BN, :].bitcast(F32)[:, bass.ds((j & 1) * (ROW // 2) + SCALE_AT + 1, 1)]
                V.scalar_tensor_tensor(rowbuf[0:BN, bass.ds(half + D, D)], hcur[0:BN, bass.ds(j * D, D)], c,
                                       rowbuf[0:BN, bass.ds(half, D)], ALU.mult, ALU.subtract
                                       ).then_inc(lo_ready, 1)

            def statistics(l, j):
                g = l * NB + j
                dve.wait_ge(hT_ready, g + 1)
                for c in range(KC):
                    last = V.bn_stats(bnst[:, c, bass.ds(j * 6, 6)], ps_t[:, c * BN:(c + 1) * BN])
                last.then_inc(stats_done, 1)

            def first_pass(i):
                if live(i):
                    scale_rows(0, i)
                if live(i - 1):
                    statistics(0, i - 1)
                    low_part(0, i - 1)

            pipeline(dve, first_pass, 1, 2)

            def scale_weights(k):
                v_eps, root, rstd, s, t, newton = (sc4[:, n, :] for n in range(6))
                dve.wait_ge(stats_done, (k + 1) * NB)
                for c in range(KC):
                    last = V.bn_aggr(mv[:, c, :], bnst[:, c, :])
                link(last)
                V.tensor_scalar(v_eps, mv[:, :, 1], BN_EPS, None, ALU.add).then_inc(bn_var, 1)
                dve.wait_ge(bn_root, k + 1)
                link(V.reciprocal(rstd, root))
                refine(rstd, v_eps, newton)
                dve.wait_ge(small_loaded, 3 * 16)
                cols = slice(k * KC, (k + 1) * KC)
                link(V.tensor_tensor(s, rstd, gb[:, 0, cols], ALU.mult))
                link(V.tensor_tensor(t, mv[:, :, 0], s, ALU.mult))
                V.tensor_tensor(t, gb[:, 1, cols], t, ALU.subtract).then_inc(bn_shift, 1)
                dve.wait_ge(wo_loaded, (k + 1) * 16)
                if k:
                    dve.wait_ge(y_done, k * NB)
                for c in range(KC):
                    last = V.tensor_scalar(wo_s[:, c, :], wo[:, c, :], s[:, c:c + 1], None, ALU.mult)
                last.then_inc(ws_ready, 1)
                dve.wait_ge(const_done, k + 1)
                link(V.tensor_tensor(const_bc[0:BN, :], const_bc[0:BN, :], ps_c[0:BN, :], ALU.add))

            def step_matrices(l, j):
                lo = dve.value_load(ends[0:1, bass.ds(j, 1)], min_val=0, max_val=STEPS - 1)
                hi = dve.value_load(ends[0:1, bass.ds(j + 1, 1)], min_val=1, max_val=STEPS)
                with dve.Fori(lo, hi) as p:
                    dve.wait_ge(landed, p + (l * STEPS + 1))
                    dve.wait_ge(steps_done, p + (l * STEPS + 1 + RING - SRING))
                    V.tensor_scalar(smat[:, bass.ds((p & (SRING - 1)) * P, P)], iota_l[:, :],
                                    dloc[:, bass.ds(p, 1)],
                                    ring[:, :].bitcast(F32)[:, bass.ds((p & (RING - 1)) * (ROW // 2) + SCALE_AT, 1)],
                                    ALU.is_equal, ALU.mult).then_inc(s_ready, 1)

            def layer_round(l):
                def run(i):
                    if live(i):
                        step_matrices(l, i)
                    if live(i - 1):
                        q = l * NB + i - 1
                        dve.wait_ge(agg_done, q + 1)
                        wait(dve, u_turned, q)
                        V.tensor_tensor(u_sb[0:BN, :], agg[0:BN, bass.ds(((i - 1) & 1) * D, D)],
                                        hcur[0:BN, bass.ds((i - 1) * D, D)], ALU.add).then_inc(u_ready, 1)
                    if live(i - 3) and l < L - 1:
                        scale_rows(l + 1, i - 3)
                    if live(i - 2):
                        j = i - 2
                        q = l * NB + j
                        dve.wait_ge(z_done, q + 1)
                        dve.wait_ge(h_turned, q + NB)
                        if not isinstance(j, int) or j > 0 or l > 0:
                            dve.wait_ge(h_ready, q + NB)
                        if isinstance(j, int) and j == 0:
                            dve.wait_ge(b_loaded, 16 * (l + 1))
                        V.scalar_tensor_tensor(h_sb[0:BN, :], ps_z[0:BN, :], dinv[0:BN, bass.ds(j, 1)],
                                               bias_bc[0:BN, :], ALU.mult, ALU.add).then_inc(z_ready, 1)
                    if live(i - 3):
                        statistics(l + 1, i - 3)
                    if live(i - 1):
                        q = l * NB + i - 1
                        dve.wait_ge(y_done, q + 1)
                        dve.wait_ge(y_loaded, q * 16 + 16)
                        wait(dve, y_stored, q * 16 - 16)
                        half = ((i - 1) & 1) * D
                        V.tensor_tensor(y_out[0:BN, bass.ds(half, D)], ps_y[0:BN, bass.ds(half, D)], y_in[0:BN, bass.ds(half, D)],
                                        ALU.add).then_inc(y_ready, 1)
                    if live(i - 3) and l < L - 1:
                        low_part(l + 1, i - 3)
                return run

            for l in range(L):
                scale_weights(l)
                pipeline(dve, layer_round(l), 3)
            scale_weights(L)

            def last_pass(j):
                q = L * NB + j
                half = (j & 1) * D
                dve.wait_ge(y_done, q + 1)
                dve.wait_ge(y_loaded, q * 16 + 16)
                V.tensor_tensor(y_in[0:BN, bass.ds(half, D)], y_in[0:BN, bass.ds(half, D)], const_bc[0:BN, :],
                                ALU.add).then_inc(out_part, 1)
                dve.wait_ge(out_part, j + 1)
                dve.wait_ge(y_stored, q * 16 - 16)
                V.tensor_tensor(y_out[0:BN, bass.ds(half, D)], ps_y[0:BN, bass.ds(half, D)], y_in[0:BN, bass.ds(half, D)],
                                ALU.add).then_inc(y_ready, 1)

            pipeline(dve, last_pass, 0)

        @block.tensor
        def _(pe):
            T = nc.tensor
            pe.sem_inc(eq_used, 2)
            pe.sem_inc(steps_done, RING)
            pe.wait_ge(consts, 3)
            T.matmul(ps_c[0:EP, 0:NB], zeros[:, 0:EP], zeros[:, 0:NB], start=True, stop=False)
            with pe.Fori(0, NCH // 2) as pair:
                for n in range(2):
                    pe.wait_ge(eq_ready, pair * 2 + n + 1)
                    for t in range(HCH):
                        last = T.matmul(ps_c[0:BN, 0:NB], eq_lane[:, n, :, t], eq_blk[:, n, :, t],
                                        start=False, stop=False)
                    last.then_inc(eq_used, 1)
            T.matmul(ps_c[0:EP, 0:NB], zeros[:, 0:EP], zeros[:, 0:NB], start=False, stop=True
                     ).then_inc(hist_done, 1)
            pe.wait_ge(hist_copied, 1)
            T.matmul(ps_c[:, 64:64 + NB + 1], ones[0:EP, :], hist[:, :], start=True, stop=True
                     ).then_inc(cnt_done, 1)
            pe.wait_ge(flag_ready, 1)
            with pe.If(pe.value_load(unsorted[0:1, 0:1], min_val=0, max_val=1) > 0):
                scan_end = wo_s[0:EP, :, :].rearrange("p c n -> p (c n)")[:, 2 * EC - 1:2 * EC]
                with pe.Fori(0, NB) as b:
                    pe.wait_ge(sort_scanned, b + 1)
                    T.matmul(ps_z[0:EP, 0:1], upper[:, :], scan_end, start=True, stop=True
                             ).then_inc(sort_offset, 1)
            pe.wait_ge(steps_made, 1)
            for out_ps, step in ((agg, step_dst), (ps_y, step_src)):
                for c in range(SC):
                    last = T.transpose(out_ps[:, c * P:(c + 1) * P], step[:, c, :], ident[:, :])
            last.then_inc(steps_turned, 1)

            def turn_h(l, j):
                g = l * NB + j
                pe.wait_ge(h_ready, g + 1)
                wait(pe, stats_done, g)
                wait(pe, hT_ready, g)
                for c in range(KC):
                    last = T.transpose(ps_t[:, c * BN:(c + 1) * BN], h_sb[0:BN, c * P:(c + 1) * P],
                                       ident[0:BN, 0:BN])
                last.then_inc(h_turned, 1)

            pipeline(pe, lambda i: turn_h(0, i), 0, 1)

            def const_row(k):
                pe.wait_ge(bn_shift, k + 1)
                pe.wait_ge(wo_loaded, (k + 1) * 16)
                for c in range(KC):
                    last = T.matmul(ps_c[0:BN, :], sc4[:, 4, c:c + 1].to_broadcast([P, BN]), wo[:, c, :],
                                    start=(c == 0), stop=(c == KC - 1))
                last.then_inc(const_done, 1)
                pe.wait_ge(ws_ready, k + 1)

            def layer_round(l):
                def run(i):
                    if live(i):
                        q = l * NB + i
                        bank = agg[:, bass.ds((i & 1) * D, D)]
                        wait(pe, u_ready, q - 1)
                        if l == 0 and isinstance(i, int) and i == 0:
                            pe.wait_ge(tables_ready, 1)
                        lo = pe.value_load(ends[0:1, bass.ds(i, 1)], min_val=0, max_val=STEPS - 1)
                        hi = pe.value_load(ends[0:1, bass.ds(i + 1, 1)], min_val=1, max_val=STEPS)
                        T.matmul(bank, zeros[:, 0:P], zeros[:, :], start=True, stop=False)
                        with pe.Fori(lo, hi) as p:
                            s = smat[:, bass.ds((p & (SRING - 1)) * P, P)]
                            pe.wait_ge(s_ready, p + (l * STEPS + 1))
                            T.matmul(bank, s, ring[:, bass.ds((p & (RING - 1)) * ROW, D)],
                                     start=False, stop=False)
                            T.matmul(bank, s, ring[:, bass.ds((p & (RING - 1)) * ROW + D, D)],
                                     start=False, stop=False).then_inc(steps_done, 1)
                        T.matmul(bank, zeros[:, 0:P], zeros[:, :], start=False, stop=True
                                 ).then_inc(agg_done, 1)
                    if live(i - 1):
                        q = l * NB + i - 1
                        pe.wait_ge(u_ready, q + 1)
                        wait(pe, uT_ready, q)
                        for c in range(KC):
                            last = T.transpose(ps_u[:, c * BN:(c + 1) * BN], u_sb[0:BN, c * P:(c + 1) * P],
                                               ident[0:BN, 0:BN])
                        last.then_inc(u_turned, 1)
                    if live(i):
                        q = l * NB + i
                        half = i & 1
                        pe.wait_ge(hT_loaded, q * 16 + 16)
                        wait(pe, y_ready, q - 1)
                        for c in range(KC):
                            last = T.matmul(ps_y[0:BN, bass.ds(half * D, D)],
                                            hT_in[:, c * BN:(c + 1) * BN], wo_s[:, c, :],
                                            start=(c == 0), stop=(c == KC - 1))
                        last.then_inc(y_done, 1)
                    if live(i - 1):
                        q = l * NB + i - 1
                        pe.wait_ge(uT_ready, q + 1)
                        wait(pe, z_ready, q)
                        if isinstance(i, int) and i == 1:
                            pe.wait_ge(w_loaded, 16 * (l + 1))
                        for c in range(KC):
                            last = T.matmul(ps_z[0:BN, :], uT_sb[:, c * BN:(c + 1) * BN], wl[:, c, :],
                                            start=(c == 0), stop=(c == KC - 1))
                        last.then_inc(z_done, 1)
                    if live(i - 2):
                        turn_h(l + 1, i - 2)
                return run

            for l in range(L):
                const_row(l)
                pipeline(pe, layer_round(l), 3)
            const_row(L)
            with pe.Fori(0, NB // 2) as m:
                for n in range(2):
                    pe.wait_ge(h3_ready, m * 2 + n + 1)
                    pe.wait_ge(y_ready, m * 2 + (L * NB + n - 1))
                    for c in range(KC):
                        at = (n * KC + c) * BN
                        last = T.matmul(ps_y[0:BN, n * D:(n + 1) * D], hT_in[:, at:at + BN], wo_s[:, c, :],
                                        start=(c == 0), stop=(c == KC - 1))
                    last.then_inc(y_done, 1)

        @block.scalar
        def _(act):
            A = nc.scalar
            with nc.allow_non_contiguous_dma(reason="2 x 2048 words, once"):
                act.dma_start(gb[:, 0, :], gamma.rearrange("(k p) -> p k", p=P)).then_inc(small_loaded, 16)
                act.dma_start(gb[:, 1, :], beta.rearrange("(k p) -> p k", p=P)).then_inc(small_loaded, 16)
            act.dma_start(const_bc[0:BN, :], bass.AP(out_b.tensor, 0, [[0, BN], [1, D]])
                          ).then_inc(small_loaded, 16)
            act.dma_start(wo[:, :, :], out_w_v[0]).then_inc(wo_loaded, 16)
            act.wait_ge(deg_ready, 1)
            A.activation(ln_r[0:BN, 1, :], dinv[0:BN, :], ACT.Sqrt).then_inc(root_ready, 1)
            act.wait_ge(deg_ready, 2)
            A.activation(ln_r[0:BN, 1, :], ln_r[0:BN, 0, :], ACT.Sqrt).then_inc(root_ready, 1)

            def high_part(l, j):
                g = l * NB + j
                half = (j & 1) * ROW
                act.wait_ge(hp_ready, g + 1)
                c = rowbuf[0:BN, :].bitcast(F32)[:, bass.ds((j & 1) * (ROW // 2) + SCALE_AT + 1, 1)]
                A.activation(rowbuf[0:BN, bass.ds(half, D)], hcur[0:BN, bass.ds(j * D, D)], ACT.Copy, scale=c
                             ).then_inc(hi_ready, 1)

            def store_rows(l, j):
                g = l * NB + j
                act.wait_ge(lo_ready, g + 1)
                wait(act, rows_stored, g * 16)
                act.dma_start(row_table[l % 2][bass.ds(j * P, P), :], rowbuf[:, bass.ds((j & 1) * ROW, ROW)]
                              ).then_inc(rows_stored, 16)

            def keep_hT(l, j):
                g = l * NB + j
                act.wait_ge(h_turned, g + 1)
                if l == L:
                    A.activation(hcur[:, bass.ds(j * D, KC * BN)], ps_t[:, 0:KC * BN], ACT.Copy
                                 ).then_inc(hT_ready, 1)
                    return
                half = (j & 1) * (KC * BN)
                wait(act, hT_stored, g * 16 - 16)
                A.activation(hT_out[:, bass.ds(half, KC * BN)], ps_t[:, 0:KC * BN], ACT.Copy
                             ).then_inc(hT_ready, 1)
                act.wait_ge(hT_ready, g + 1)
                wait(act, hT_stored, g * 16)
                act.dma_start(hT_dram[l % 2][bass.ds(j, 1), :, :].rearrange("o p n -> (o p) n"),
                              hT_out[:, bass.ds(half, KC * BN)]).then_inc(hT_stored, 16)

            def first_pass(i):
                if live(i):
                    wait(act, hp_ready, i)
                    wait(act, h_turned, i)
                    A.activation(h_sb[0:BN, :], hcur[0:BN, bass.ds(i * D, D)], ACT.Relu,
                                 bias=ln_r[0:BN, 3, bass.ds(i, 1)], scale=ln_r[0:BN, 2, bass.ds(i, 1)]
                                 ).then_inc(h_ready, 1)
                if live(i - 1):
                    high_part(0, i - 1)
                    keep_hT(0, i - 1)
                    store_rows(0, i - 1)

            act.wait_ge(ln_ready, 1)
            pipeline(act, first_pass, 1, 3)

            def load_y(l, j):
                q = l * NB + j
                wait(act, y_loaded, q * 16)
                wait(act, y_ready, q - 1)
                at = bass.ds((j & 1) * D, D)
                if l == 0:
                    act.dma_start(y_in[0:BN, at], x_v[bass.ds(j, 1), :, :].rearrange("o p n -> (o p) n")
                                  ).then_inc(y_loaded, 16)
                else:
                    act.dma_start(y_in[:, at], y_dram[bass.ds(j, 1), :, :].rearrange("o p n -> (o p) n")
                                  ).then_inc(y_loaded, 16)

            def layer_start(l):
                if l < L:
                    wait(act, z_done, l * NB)
                    act.dma_start(wl[:, :, :], w_v[l]).then_inc(w_loaded, 16)
                    wait(act, z_ready, l * NB)
                    act.dma_start(bias_bc[0:BN, :], bass.AP(bs.tensor, l * D, [[0, BN], [1, D]])
                                  ).then_inc(b_loaded, 16)
                    act.wait_ge(hT_stored, 16 * NB * (l + 1))
                wait(act, y_stored, 16 * NB * l)
                act.wait_ge(bn_var, l + 1)
                A.activation(sc4[:, 1, :], sc4[:, 0, :], ACT.Sqrt).then_inc(bn_root, 1)
                if l < L:
                    act.wait_ge(ws_ready, l + 1)
                    act.wait_ge(const_done, l + 1)
                    act.dma_start(wo[:, :, :], out_w_v[l + 1]).then_inc(wo_loaded, 16)

            def layer_round(l):
                def run(i):
                    if live(i):
                        q = l * NB + i
                        wait(act, y_done, q)
                        act.dma_start(hT_in[:, 0:KC * BN],
                                      hT_dram[l % 2][bass.ds(i, 1), :, :].rearrange("o p n -> (o p) n")
                                      ).then_inc(hT_loaded, 16)
                        load_y(l, i)
                    if live(i - 3) and l < L - 1:
                        high_part(l + 1, i - 3)
                    if live(i - 3):
                        keep_hT(l + 1, i - 3)
                    if live(i - 2):
                        q = l * NB + i - 2
                        act.wait_ge(z_ready, q + 1)
                        A.activation(h_sb[0:BN, :], h_sb[0:BN, :], ACT.Gelu).then_inc(h_ready, 1)
                    if live(i - 1):
                        q = l * NB + i - 1
                        act.wait_ge(u_turned, q + 1)
                        wait(act, z_done, q)
                        A.activation(uT_sb[:, :], ps_u[:, 0:KC * BN], ACT.Copy).then_inc(uT_ready, 1)
                    if live(i - 3) and l < L - 1:
                        store_rows(l + 1, i - 3)
                    if live(i - 1):
                        q = l * NB + i - 1
                        act.wait_ge(y_ready, q + 1)
                        wait(act, y_stored, q * 16)
                        act.dma_start(y_dram[bass.ds(i - 1, 1), :, :].rearrange("o p n -> (o p) n"),
                                      y_out[:, bass.ds(((i - 1) & 1) * D, D)]).then_inc(y_stored, 16)
                return run

            act.wait_ge(tables_ready, 1)
            for l in range(L):
                layer_start(l)
                pipeline(act, layer_round(l), 3)
            layer_start(L)

            def last_pass(i):
                if live(i):
                    load_y(L, i)
                    act.wait_ge(y_done, L * NB + i - 1)
                    A.activation(hT_in[:, bass.ds((i & 1) * (KC * BN), KC * BN)],
                                 hcur[:, bass.ds(i * D, KC * BN)], ACT.Copy).then_inc(h3_ready, 1)
                if live(i - 1):
                    q = L * NB + i - 1
                    act.wait_ge(y_ready, q + 1)
                    act.wait_ge(y_stored, q * 16)
                    act.dma_start(out_v[bass.ds(i - 1, 1), :, :].rearrange("o p n -> (o p) n"),
                                  y_out[0:BN, bass.ds(((i - 1) & 1) * D, D)]).then_inc(y_stored, 16)

            act.wait_ge(hT_ready, (L + 1) * NB)
            pipeline(act, last_pass, 1)
            act.wait_ge(y_stored, (L + 1) * NB * 16)


_INS = ['x', 'src', 'dst', 'L0_gnn_Ws', 'L0_gnn_bs', 'L0_gnn_bn_gamma', 'L0_gnn_bn_beta', 'L0_gnn_out_W',
        'L0_gnn_out_b']
_OUTS = [((6250, 512), 'float32')]


def kernel(**inputs):
    import numpy as _np
    import concourse.bacc as _bacc
    from concourse import mybir as _mybir
    from concourse.bass_utils import run_bass_kernel_spmd as _run

    nc = _bacc.Bacc("TRN2", target_bir_lowering=False, num_devices=1)
    arrays, args = {}, []
    for name in _INS:
        a = _np.ascontiguousarray(inputs[name])
        arrays[f"in_{name}_dram"] = a
        args.append(nc.dram_tensor(f"in_{name}_dram", a.shape, _mybir.dt.from_np(a.dtype), kind="ExternalInput").ap())
    for i, (shape, dtype) in enumerate(_OUTS):
        dt = _mybir.dt.from_np(_np.dtype(dtype))
        args.append(nc.dram_tensor(f"out_{i}_dram", shape, dt, kind="ExternalOutput").ap())
    gnn_kernel(nc, *args)
    r = _run(nc, [arrays], core_ids=[0])
    got = tuple(r.results[0][f"out_{i}_dram"] for i in range(len(_OUTS)))
    return got[0]
```
